# Optimizing a Trainium2 kernel written in Bass

```python
import numpy as np
import jax
import jax.numpy as jnp

def _softmax(x, axis=-1):
    return jax.nn.softmax(x, axis=axis)

def _gelu(x):
    return jax.nn.gelu(x, approximate=True)

def _silu(x):
    return jax.nn.silu(x)

def _sigmoid(x):
    return jax.nn.sigmoid(x)

def _layernorm(x, axis=-1, eps=1e-05):
    m = jnp.mean(x, axis=axis, keepdims=True)
    v = jnp.var(x, axis=axis, keepdims=True)
    return (x - m) / jnp.sqrt(v + eps)

def _scatter_add(tgt, idx, src, axis=0):
    return tgt.at[idx].add(src)

def _segment_sum(src, seg, n):
    return jax.ops.segment_sum(src, seg, n)
kernel_name = 'mk_dlrm_tower_d1_rec_r8_1d3df1'

def setup_inputs(seed: int=0):
    np.random.seed(seed)
    _w = jnp.asarray

    def _rec_inputs():
        import jax
        import jax.numpy as jnp
        _tk = jax.random.key(seed)
        dense_ctx = jax.random.normal(jax.random.fold_in(_tk, 190), (1024, 16), jnp.float32)
        ids = jnp.stack([jax.random.randint(jax.random.fold_in(_tk, 200 + f), (1024,), 0, v, jnp.int32) for f, v in enumerate([125000, 125000, 1000, 1250, 12500, 1250, 12500, 12500, 125000, 125000, 1000, 125000, 125000, 1000, 1250, 125000, 1000, 1250, 12500, 12500, 12500, 1250, 1250, 1250, 1250, 12500, 12500, 12500, 12500, 1250, 1000, 1250, 12500, 1250, 12500, 1250, 12500, 12500, 1000])], axis=1)
        tbl_0 = 0.05 * jax.random.normal(jax.random.fold_in(_tk, 500 + 0), (125000, 16), jnp.float32)
        tbl_1 = 0.05 * jax.random.normal(jax.random.fold_in(_tk, 500 + 1), (125000, 16), jnp.float32)
        tbl_2 = 0.05 * jax.random.normal(jax.random.fold_in(_tk, 500 + 2), (1000, 16), jnp.float32)
        tbl_3 = 0.05 * jax.random.normal(jax.random.fold_in(_tk, 500 + 3), (1250, 16), jnp.float32)
        tbl_4 = 0.05 * jax.random.normal(jax.random.fold_in(_tk, 500 + 4), (12500, 16), jnp.float32)
        tbl_5 = 0.05 * jax.random.normal(jax.random.fold_in(_tk, 500 + 5), (1250, 16), jnp.float32)
        tbl_6 = 0.05 * jax.random.normal(jax.random.fold_in(_tk, 500 + 6), (12500, 16), jnp.float32)
        tbl_7 = 0.05 * jax.random.normal(jax.random.fold_in(_tk, 500 + 7), (12500, 16), jnp.float32)
        tbl_8 = 0.05 * jax.random.normal(jax.random.fold_in(_tk, 500 + 8), (125000, 16), jnp.float32)
        tbl_9 = 0.05 * jax.random.normal(jax.random.fold_in(_tk, 500 + 9), (125000, 16), jnp.float32)
        tbl_10 = 0.05 * jax.random.normal(jax.random.fold_in(_tk, 500 + 10), (1000, 16), jnp.float32)
        tbl_11 = 0.05 * jax.random.normal(jax.random.fold_in(_tk, 500 + 11), (125000, 16), jnp.float32)
        tbl_12 = 0.05 * jax.random.normal(jax.random.fold_in(_tk, 500 + 12), (125000, 16), jnp.float32)
        tbl_13 = 0.05 * jax.random.normal(jax.random.fold_in(_tk, 500 + 13), (1000, 16), jnp.float32)
        tbl_14 = 0.05 * jax.random.normal(jax.random.fold_in(_tk, 500 + 14), (1250, 16), jnp.float32)
        tbl_15 = 0.05 * jax.random.normal(jax.random.fold_in(_tk, 500 + 15), (125000, 16), jnp.float32)
        tbl_16 = 0.05 * jax.random.normal(jax.random.fold_in(_tk, 500 + 16), (1000, 16), jnp.float32)
        tbl_17 = 0.05 * jax.random.normal(jax.random.fold_in(_tk, 500 + 17), (1250, 16), jnp.float32)
        tbl_18 = 0.05 * jax.random.normal(jax.random.fold_in(_tk, 500 + 18), (12500, 16), jnp.float32)
        tbl_19 = 0.05 * jax.random.normal(jax.random.fold_in(_tk, 500 + 19), (12500, 16), jnp.float32)
        tbl_20 = 0.05 * jax.random.normal(jax.random.fold_in(_tk, 500 + 20), (12500, 16), jnp.float32)
        tbl_21 = 0.05 * jax.random.normal(jax.random.fold_in(_tk, 500 + 21), (1250, 16), jnp.float32)
        tbl_22 = 0.05 * jax.random.normal(jax.random.fold_in(_tk, 500 + 22), (1250, 16), jnp.float32)
        tbl_23 = 0.05 * jax.random.normal(jax.random.fold_in(_tk, 500 + 23), (1250, 16), jnp.float32)
        tbl_24 = 0.05 * jax.random.normal(jax.random.fold_in(_tk, 500 + 24), (1250, 16), jnp.float32)
        tbl_25 = 0.05 * jax.random.normal(jax.random.fold_in(_tk, 500 + 25), (12500, 16), jnp.float32)
        tbl_26 = 0.05 * jax.random.normal(jax.random.fold_in(_tk, 500 + 26), (12500, 16), jnp.float32)
        tbl_27 = 0.05 * jax.random.normal(jax.random.fold_in(_tk, 500 + 27), (12500, 16), jnp.float32)
        tbl_28 = 0.05 * jax.random.normal(jax.random.fold_in(_tk, 500 + 28), (12500, 16), jnp.float32)
        tbl_29 = 0.05 * jax.random.normal(jax.random.fold_in(_tk, 500 + 29), (1250, 16), jnp.float32)
        tbl_30 = 0.05 * jax.random.normal(jax.random.fold_in(_tk, 500 + 30), (1000, 16), jnp.float32)
        tbl_31 = 0.05 * jax.random.normal(jax.random.fold_in(_tk, 500 + 31), (1250, 16), jnp.float32)
        tbl_32 = 0.05 * jax.random.normal(jax.random.fold_in(_tk, 500 + 32), (12500, 16), jnp.float32)
        tbl_33 = 0.05 * jax.random.normal(jax.random.fold_in(_tk, 500 + 33), (1250, 16), jnp.float32)
        tbl_34 = 0.05 * jax.random.normal(jax.random.fold_in(_tk, 500 + 34), (12500, 16), jnp.float32)
        tbl_35 = 0.05 * jax.random.normal(jax.random.fold_in(_tk, 500 + 35), (1250, 16), jnp.float32)
        tbl_36 = 0.05 * jax.random.normal(jax.random.fold_in(_tk, 500 + 36), (12500, 16), jnp.float32)
        tbl_37 = 0.05 * jax.random.normal(jax.random.fold_in(_tk, 500 + 37), (12500, 16), jnp.float32)
        tbl_38 = 0.05 * jax.random.normal(jax.random.fold_in(_tk, 500 + 38), (1000, 16), jnp.float32)
        _rk = jax.random.fold_in(_tk, 7)
        W_top1 = 0.05 * jax.random.normal(jax.random.fold_in(_tk, 801), (400, 512), jnp.float32)
        W_top2 = 0.0441942 * jax.random.normal(jax.random.fold_in(_tk, 802), (512, 256), jnp.float32)
        W_top3 = 0.0625 * jax.random.normal(jax.random.fold_in(_tk, 803), (256, 1), jnp.float32)
        b_top1 = jnp.zeros((512,), jnp.float32)
        b_top2 = jnp.zeros((256,), jnp.float32)
        return (dense_ctx, ids, tbl_0, tbl_1, tbl_2, tbl_3, tbl_4, tbl_5, tbl_6, tbl_7, tbl_8, tbl_9, tbl_10, tbl_11, tbl_12, tbl_13, tbl_14, tbl_15, tbl_16, tbl_17, tbl_18, tbl_19, tbl_20, tbl_21, tbl_22, tbl_23, tbl_24, tbl_25, tbl_26, tbl_27, tbl_28, tbl_29, tbl_30, tbl_31, tbl_32, tbl_33, tbl_34, tbl_35, tbl_36, tbl_37, tbl_38, W_top1, b_top1, W_top2, b_top2, W_top3)
    dense_ctx, ids, tbl_0, tbl_1, tbl_2, tbl_3, tbl_4, tbl_5, tbl_6, tbl_7, tbl_8, tbl_9, tbl_10, tbl_11, tbl_12, tbl_13, tbl_14, tbl_15, tbl_16, tbl_17, tbl_18, tbl_19, tbl_20, tbl_21, tbl_22, tbl_23, tbl_24, tbl_25, tbl_26, tbl_27, tbl_28, tbl_29, tbl_30, tbl_31, tbl_32, tbl_33, tbl_34, tbl_35, tbl_36, tbl_37, tbl_38, W_top1, b_top1, W_top2, b_top2, W_top3 = _rec_inputs()

    def _L0_rec_setup():
        import jax, jax.numpy as jnp
        import numpy as np
        B, F0, D = (256, 39, 16)
        CROSS = [128, 128, 128]
        key = jax.random.key(seed)
        k0, k1, k2, k3 = jax.random.split(key, 4)
        inputs = jax.random.normal(k0, (B, F0, D), dtype=jnp.float32)
        f0 = jax.random.normal(k1, (F0 * F0, CROSS[0]), dtype=jnp.float32) * 0.05
        f1 = jax.random.normal(k2, (CROSS[0] * F0, CROSS[1]), dtype=jnp.float32) * 0.05
        f2 = jax.random.normal(k3, (CROSS[1] * F0, CROSS[2]), dtype=jnp.float32) * 0.05
        return {'inputs': inputs, 'f0': f0, 'f1': f1, 'f2': f2}
    _L0_rec_all = _L0_rec_setup()
    _L0_rec_in = {k: v for k, v in _L0_rec_all.items() if k in ('f0', 'f1', 'f2')}
    del _L0_rec_all
    return {'dense_ctx': dense_ctx, 'ids': ids, 'tbl_0': tbl_0, 'tbl_1': tbl_1, 'tbl_2': tbl_2, 'tbl_3': tbl_3, 'tbl_4': tbl_4, 'tbl_5': tbl_5, 'tbl_6': tbl_6, 'tbl_7': tbl_7, 'tbl_8': tbl_8, 'tbl_9': tbl_9, 'tbl_10': tbl_10, 'tbl_11': tbl_11, 'tbl_12': tbl_12, 'tbl_13': tbl_13, 'tbl_14': tbl_14, 'tbl_15': tbl_15, 'tbl_16': tbl_16, 'tbl_17': tbl_17, 'tbl_18': tbl_18, 'tbl_19': tbl_19, 'tbl_20': tbl_20, 'tbl_21': tbl_21, 'tbl_22': tbl_22, 'tbl_23': tbl_23, 'tbl_24': tbl_24, 'tbl_25': tbl_25, 'tbl_26': tbl_26, 'tbl_27': tbl_27, 'tbl_28': tbl_28, 'tbl_29': tbl_29, 'tbl_30': tbl_30, 'tbl_31': tbl_31, 'tbl_32': tbl_32, 'tbl_33': tbl_33, 'tbl_34': tbl_34, 'tbl_35': tbl_35, 'tbl_36': tbl_36, 'tbl_37': tbl_37, 'tbl_38': tbl_38, 'W_top1': W_top1, 'b_top1': b_top1, 'W_top2': W_top2, 'b_top2': b_top2, 'W_top3': W_top3, 'L0_rec_f0': _L0_rec_in['f0'], 'L0_rec_f1': _L0_rec_in['f1'], 'L0_rec_f2': _L0_rec_in['f2']}

def reference(dense_ctx, ids, tbl_0, tbl_1, tbl_2, tbl_3, tbl_4, tbl_5, tbl_6, tbl_7, tbl_8, tbl_9, tbl_10, tbl_11, tbl_12, tbl_13, tbl_14, tbl_15, tbl_16, tbl_17, tbl_18, tbl_19, tbl_20, tbl_21, tbl_22, tbl_23, tbl_24, tbl_25, tbl_26, tbl_27, tbl_28, tbl_29, tbl_30, tbl_31, tbl_32, tbl_33, tbl_34, tbl_35, tbl_36, tbl_37, tbl_38, W_top1, b_top1, W_top2, b_top2, W_top3, L0_rec_f0, L0_rec_f1, L0_rec_f2):
    import jax
    import jax.numpy as jnp

    def _L0_rec_ref(inputs, f0, f1, f2):
        import jax, jax.numpy as jnp
        import numpy as np
        B, F0, D = (256, 39, 16)
        CROSS = [128, 128, 128]
        filters = [f0, f1, f2]
        x0 = inputs
        xk = inputs
        outs = []
        for W in filters:
            b, f, d = x0.shape
            g = xk.shape[1]
            z = jnp.einsum('bfd,bgd->bfgd', x0, xk).reshape(b, f * g, d)
            cur = jnp.einsum('bpd,pm->bmd', z, W)
            outs.append(cur)
            xk = cur
        result = jnp.concatenate(outs, axis=1)
        return jnp.sum(result, axis=-1)
    e = jnp.stack([tbl_0[ids[:, 0]], tbl_1[ids[:, 1]], tbl_2[ids[:, 2]], tbl_3[ids[:, 3]], tbl_4[ids[:, 4]], tbl_5[ids[:, 5]], tbl_6[ids[:, 6]], tbl_7[ids[:, 7]], tbl_8[ids[:, 8]], tbl_9[ids[:, 9]], tbl_10[ids[:, 10]], tbl_11[ids[:, 11]], tbl_12[ids[:, 12]], tbl_13[ids[:, 13]], tbl_14[ids[:, 14]], tbl_15[ids[:, 15]], tbl_16[ids[:, 16]], tbl_17[ids[:, 17]], tbl_18[ids[:, 18]], tbl_19[ids[:, 19]], tbl_20[ids[:, 20]], tbl_21[ids[:, 21]], tbl_22[ids[:, 22]], tbl_23[ids[:, 23]], tbl_24[ids[:, 24]], tbl_25[ids[:, 25]], tbl_26[ids[:, 26]], tbl_27[ids[:, 27]], tbl_28[ids[:, 28]], tbl_29[ids[:, 29]], tbl_30[ids[:, 30]], tbl_31[ids[:, 31]], tbl_32[ids[:, 32]], tbl_33[ids[:, 33]], tbl_34[ids[:, 34]], tbl_35[ids[:, 35]], tbl_36[ids[:, 36]], tbl_37[ids[:, 37]], tbl_38[ids[:, 38]]], axis=1)
    z = _L0_rec_ref(e, L0_rec_f0, L0_rec_f1, L0_rec_f2)
    z = z.reshape(z.shape[0], -1)
    h = jnp.concatenate([z, dense_ctx], axis=1)
    h = jnp.maximum(h @ W_top1 + b_top1, 0.0)
    h = jnp.maximum(h @ W_top2 + b_top2, 0.0)
    y = h @ W_top3
    return y

_drawn_inputs = setup_inputs


def setup_inputs(seed=0):
    import zlib

    import numpy as np

    out = dict(_drawn_inputs(seed))
    spreads = {'b_top1': (0.0, 0.56), 'b_top2': (0.0, 0.1)}
    factors = {'tbl_0': 4.689,
     'tbl_1': 4.862,
     'tbl_2': 4.55,
     'tbl_3': 4.876,
     'tbl_4': 4.749,
     'tbl_5': 5.026,
     'tbl_6': 4.549,
     'tbl_7': 4.789,
     'tbl_8': 5.038,
     'tbl_9': 4.419,
     'tbl_10': 5.036,
     'tbl_11': 4.517,
     'tbl_12': 4.249,
     'tbl_13': 4.367,
     'tbl_14': 4.611,
     'tbl_15': 4.656,
     'tbl_16': 5.109,
     'tbl_17': 4.717,
     'tbl_18': 4.823,
     'tbl_19': 4.938,
     'tbl_20': 4.78,
     'tbl_21': 4.613,
     'tbl_22': 4.594,
     'tbl_23': 4.616,
     'tbl_24': 4.382,
     'tbl_25': 4.59,
     'tbl_26': 4.629,
     'tbl_27': 5.075,
     'tbl_28': 4.894,
     'tbl_29': 4.816,
     'tbl_30': 5.015,
     'tbl_31': 4.538,
     'tbl_32': 4.79,
     'tbl_33': 4.511,
     'tbl_34': 4.458,
     'tbl_35': 4.572,
     'tbl_36': 4.677,
     'tbl_37': 4.864,
     'tbl_38': 4.829,
     'L0_rec_f1': 5.093,
     'L0_rec_f2': 8.0}
    for name, (base, spread) in spreads.items():
        noise = np.random.default_rng([zlib.crc32(name.encode()), seed]).standard_normal(out[name].shape)
        drawn = base * np.exp(spread * noise) if base else spread * noise
        out[name] = jnp.asarray(drawn.astype(out[name].dtype))
    for name, factor in factors.items():
        out[name] = (out[name] * factor).astype(out[name].dtype)
    return out
```

```python
import numpy as np
import concourse.bass as bass
from concourse import mybir
from concourse.alu_op_type import AluOpType as ALU
from contextlib import ExitStack

FP32 = mybir.dt.float32
F32R = mybir.dt.float32r
INT32 = mybir.dt.int32
ACT = mybir.ActivationFunctionType
AX = mybir.AxisListType

P = 128
B, F, D, M, DENSE = 1024, 39, 16, 128, 16
H1, H2 = 512, 256
GROUPS = B // P
TILES = D
TQ = 4
QUADS = TILES // TQ
COLS = TQ * P
ROT = F // 2 + 1
RPC = 3
CHUNKS = -(-ROT // RPC)
FPB = 4
BANKS = -(-F // FPB)
RING = 4
SLOTS = TILES * BANKS
ACT_BANKS = (1, 4, 7, 9)
BLK = 8
NBLK = P // BLK
FX = F + 1


def bank_features(u):
    return range(FPB * u, min(F, FPB * u + FPB))


def features_of(act, banks=BANKS):
    return sum(len(bank_features(u)) for u in range(banks) if (u in ACT_BANKS) == act)


NA = features_of(True)
ND = features_of(False)
SUMS = NA + 2

T_SLOT, XT_SLOT, A_SLOT, AC_SLOT = 1, 2, 4, 5
B_SLOT = [7 + 3 * c for c in range(CHUNKS)]
X1H_SLOT, X1L_SLOT, S0_SLOT = 32, 34, 35
P2_SLOT = [24 + 5 * t for t in range(NBLK)]
S2_SLOT, S2_PER_SLOT = 104, 2
DT_SLOT = 20
MLP1_SLOT, MLP2_SLOT, MLP3_SLOT = 127, 136, 143
S0_COPY_SLOT = 140
XS_HI_SLOT, XS_LO_SLOT = 112, 115
GATHERS_PER_TILE = 4


def rows_of(c):
    return F * min(RPC, ROT - RPC * c)


def build(nc, ids, dense, tables, w0, w1, w2, wt1, bt1, wt2, bt2, wt3, c_ident, c_sel, c_mask, y):
    ctx = ExitStack()
    with ctx:
        def sb(name, shape, dt=FP32):
            return ctx.enter_context(nc.sbuf_tensor(name, shape, dt))

        def pb(name, shape):
            return ctx.enter_context(nc.psum_tensor(name, shape, FP32))

        def sem(name):
            return ctx.enter_context(nc.semaphore(name))

        ident = sb("ident", [P, P])
        sel = sb("sel", [2 * F, 1 + CHUNKS, RPC * F], F32R)
        mask = sb("mask", [P, BLK])
        v_hi = sb("v_hi", [RPC * F, CHUNKS, M], F32R)
        v_lo = sb("v_lo", [RPC * F, CHUNKS, M], F32R)
        w1_hi = sb("w1_hi", [M, F * M], F32R)
        w1_lo = sb("w1_lo", [M, F * M], F32R)
        w2_sb = sb("w2_sb", [M, F, M])
        wt1_sb = sb("wt1_sb", [P, 4, H1])
        wt2_sb = sb("wt2_sb", [P, H1 // P, H2])
        wt3_sb = sb("wt3_sb", [P, H2 // P])
        bt1_sb = sb("bt1_sb", [P, H1 // P])
        bt2_sb = sb("bt2_sb", [P, H2 // P])
        ids_all = sb("ids_all", [P, GROUPS, F], INT32)
        ids_sb = sb("ids_sb", [P, F], INT32)
        xg = sb("xg", [P, F * D])
        x_dve = sb("x_dve", [P, D, F])
        x_act = sb("x_act", [P, D, FX])
        xs = sb("xs", [P, D, 2 * F])
        xt = sb("xt", [2 * F, COLS], F32R)
        a_sb = sb("a_sb", [RPC * F, COLS])
        z = sb("z", [RPC * F, 2, COLS])
        z_hi = sb("z_hi", [RPC * F, 2, COLS], F32R)
        z_lo = sb("z_lo", [RPC * F, 2, COLS], F32R)
        x1_hi = sb("x1_hi", [M, 2, COLS], F32R)
        x1_lo = sb("x1_lo", [M, 2, COLS], F32R)
        parts = sb("parts", [P, 2, SUMS, M])
        x2 = sb("x2", [P, D, M])
        x2r = sb("x2r", [P, NBLK, M])
        x0r = sb("x0r", [P, NBLK, FX])
        blk = sb("blk", [P, 2, BLK, FX])
        p2 = sb("p2", [M, FX, P])
        s0_acc = sb("s0_acc", [M, P])
        s0_quad = sb("s0_quad", [M, P])
        s0_in = sb("s0_in", [M, P])
        s2_in = sb("s2_in", [M, P])
        dense_sb = sb("dense_sb", [P, DENSE])
        dense_t = sb("dense_t", [P, P])
        h1 = sb("h1", [P, H1 // P, P])
        h2 = sb("h2", [P, H2 // P, P])
        y_sb = sb("y_sb", [1, P])
        w1_stage = p2[:, 0:F, :].rearrange("g f m -> g (f m)")
        va, vb, vs = x2[0:RPC * F, 0:CHUNKS, :], x2[0:RPC * F, CHUNKS:2 * CHUNKS, :], x2r[0:RPC * F, 0:CHUNKS, :]
        sel_stage = parts[0:2 * F, 0, 0:8, :].rearrange("p a b -> p (a b)")[:, 0:(1 + CHUNKS) * RPC * F]

        u_ps = [pb(f"u_ps{i}", [P, FPB * M]) for i in range(RING)]
        sel_ps = [pb(f"sel_ps{i}", [P, COLS]) for i in range(2)]
        x1_ps = pb("x1_ps", [M, COLS])
        post_ps = pb("post_ps", [P, 512])

        consts_in = sem("consts_in")
        v_in = sem("v_in")
        w1_in = sem("w1_in")
        w2_in = sem("w2_in")
        mlp_in = sem("mlp_in")
        ids_in = sem("ids_in")
        ids_ready = sem("ids_ready")
        passed = {"sp": sem("sp_passed"), "pool": sem("pool_passed")}
        dense_in = sem("dense_in")
        gathered = sem("gathered")
        x0r_in = sem("x0r_in")
        x2r_in = [sem(f"x2r_in{half}") for half in range(2)]
        y_out = sem("y_out")
        zeroed = sem("zeroed")
        v_prep = sem("v_prep")
        v_hi_ready = sem("v_hi_ready")
        v_lo_ready = sem("v_lo_ready")
        sel_cast = sem("sel_cast")
        w1_hi_ready = sem("w1_hi_ready")
        w1_lo_ready = sem("w1_lo_ready")
        xs_hi = sem("xs_hi")
        xs_lo = sem("xs_lo")
        x_act_ready = sem("x_act_ready")
        x_dve_ready = sem("x_dve_ready")
        xt_ready = sem("xt_ready")
        xt_copied = sem("xt_copied")
        sel_ready = sem("sel_ready")
        a_copied = sem("a_copied")
        z_ready = sem("z_ready")
        z_hi_ready = sem("z_hi_ready")
        z_lo_ready = sem("z_lo_ready")
        l0_done = sem("l0_done")
        x1_hi_ready = sem("x1_hi_ready")
        x1_lo_ready = sem("x1_lo_ready")
        s0_reduced = sem("s0_reduced")
        s0_added = sem("s0_added")
        s0_in_ready = sem("s0_in_ready")
        u_ready = sem("u_ready")
        act_part = sem("act_part")
        dve_part = sem("dve_part")
        pool_step = sem("pool_step")
        x2_ready = sem("x2_ready")
        blk_ready = sem("blk_ready")
        p2_ready = sem("p2_ready")
        p2_copied = sem("p2_copied")
        s2_ready = sem("s2_ready")
        s2_copied = sem("s2_copied")
        dt_ready = sem("dt_ready")
        dt_copied = sem("dt_copied")
        h1_ready = sem("h1_ready")
        h1_copied = sem("h1_copied")
        h2_ready = sem("h2_ready")
        h2_copied = sem("h2_copied")
        y_ready = sem("y_ready")
        y_copied = sem("y_copied")

        block = ctx.enter_context(nc.Block())

        def reach(eng, s, value):
            if not isinstance(value, int) or value > 0:
                eng.wait_ge(s, value)

        def bodies(eng, body):
            body(0)
            with eng.Fori(1, GROUPS - 1) as j:
                body(j)
            body(GROUPS - 1)

        def has_prev(j):
            return not (isinstance(j, int) and j == 0)

        def has_next(j):
            return not (isinstance(j, int) and j == GROUPS - 1)

        def next_quad(j, s):
            q, at = divmod(s, TQ * BANKS)
            if q == QUADS - 1 and not has_next(j):
                return None
            return j * QUADS + q + 1, (q + 1) % QUADS, at

        @block.sync
        def _(sp):
            sp.dma_start(ids_all[:], ids.rearrange("(j p) f -> p j f", p=P)).then_inc(ids_in, 16)
            sp.dma_start(ident[:], c_ident).then_inc(consts_in, 16)
            sp.dma_start(mask[:], c_mask).then_inc(consts_in, 16)
            sp.dma_start(sel_stage, c_sel).then_inc(consts_in, 16)
            for k in range(ROT):
                c, row = k // RPC, F * (k % RPC)
                for lo, hi, wrap in ((0, F - k, 0), (F - k, F, 1)):
                    if hi == lo:
                        continue
                    n = hi - lo
                    for dst, first in ((va, (F + 1) * lo + k - F * wrap),
                                       (vb, (F + 1) * lo + F * k - F * F * wrap)):
                        sp.dma_start(dst[row + lo:row + hi, c, :],
                                     w0[first:first + (F + 1) * (n - 1) + 1:F + 1, :]).then_inc(v_in, 16)
            sp.dma_start(w2_sb[:], w2.rearrange("(f g) m -> g f m", g=M)).then_inc(w2_in, 16)
            sp.wait_ge(zeroed, 3)
            sp.dma_start(wt1_sb[:, 0:3, :], wt1[0:3 * P, :].rearrange("(k p) n -> p k n", p=P)).then_inc(mlp_in, 16)
            sp.dma_start(wt1_sb[0:DENSE, 3, :], wt1[3 * P:3 * P + DENSE, :]).then_inc(mlp_in, 16)
            sp.dma_start(wt2_sb[:], wt2.rearrange("(k p) n -> p k n", p=P)).then_inc(mlp_in, 16)
            with nc.allow_non_contiguous_dma(reason="biases and the last layer's column, once"):
                sp.dma_start(wt3_sb[:], wt3.rearrange("(k p) n -> p (k n)", p=P)).then_inc(mlp_in, 16)
                sp.dma_start(bt1_sb[:], bt1.rearrange("(k p) -> p k", p=P)).then_inc(mlp_in, 16)
                sp.dma_start(bt2_sb[:], bt2.rearrange("(k p) -> p k", p=P)).then_inc(mlp_in, 16)

            def regroup(half, dst, src, arrived):
                rows = BLK * D // 2
                for t in range(NBLK):
                    sp.dma_start(dst[half * rows:(half + 1) * rows, t, :],
                                 src[BLK * t:BLK * (t + 1), half * D // 2:(half + 1) * D // 2, :]).then_inc(arrived, 16)

            def sp_wait(semaphore, value):
                if not isinstance(value, int) or value > 0:
                    sp.wait_ge(semaphore, value)
                    sp.sem_inc(passed["sp"], 1)

            def body(j):
                if has_prev(j):
                    sp_wait(dt_ready, j - 1)
                    sp.dma_start(dense_sb[:], dense[bass.ts(j - 1, P), :]).then_inc(dense_in, 16)
                sp_wait(x_act_ready, j + 1)
                sp_wait(blk_ready, j * NBLK * BLK)
                for half in range(2):
                    regroup(half, x0r, x_act, x0r_in)
                sp_wait(p2_ready, j * NBLK)
                sp_wait(x2_ready, j * TILES + TILES // 2)
                regroup(0, x2r, x2, x2r_in[0])
                if has_prev(j):
                    store_y(j - 1)
                sp_wait(x2_ready, (j + 1) * TILES)
                regroup(1, x2r, x2, x2r_in[1])

            def store_y(g):
                sp_wait(y_copied, g + 1)
                sp.dma_start(y[bass.ts(g, P), :].rearrange("b n -> n b"), y_sb[:]).then_inc(y_out, 16)

            bodies(sp, body)
            sp.wait_ge(dt_ready, GROUPS - 1)
            sp.dma_start(dense_sb[:], dense[(GROUPS - 1) * P:GROUPS * P, :]).then_inc(dense_in, 16)
            store_y(GROUPS - 1)
            sp.wait_ge(y_out, 16 * GROUPS)

        @block.gpsimd
        def _(pool):
            pool.memset(x_act[:], 1.0).then_inc(zeroed, 1)
            pool.memset(dense_t[:], 0.0).then_inc(zeroed, 1)
            pool.memset(wt1_sb[:, 3, :], 0.0).then_inc(zeroed, 1)

            def gather(f):
                pool.indirect_dma_start(xg[:, D * f:D * (f + 1)], None, tables[f],
                                        bass.IndirectOffsetOnAxis(ap=ids_sb[:, f:f + 1], axis=0)).then_inc(gathered, 16)

            def take_ids(g):
                reach(pool, gathered, 16 * F * g)
                src = ids_all[:, g, :] if isinstance(g, int) else ids_all[:, bass.ds(g, 1), :].rearrange("p a f -> p (a f)")
                pool.tensor_copy(ids_sb[:], src).then_inc(ids_ready, 1)
                pool.wait_ge(ids_ready, g + 1)
                pool.sem_inc(passed["pool"], 1)

            pool.wait_ge(ids_in, 16)
            take_ids(0)
            for f in range(F):
                gather(f)

            def body(j):
                for i in range(TILES):
                    if has_next(j):
                        if i == 0:
                            pool.wait_ge(x_act_ready, j + 1)
                            pool.wait_ge(x_dve_ready, j + 1)
                            pool.wait_ge(xs_hi, j + 1)
                            pool.wait_ge(xs_lo, j + 1)
                            take_ids(j + 1)
                        for f in range(GATHERS_PER_TILE * i, min(F, GATHERS_PER_TILE * (i + 1))):
                            gather(f)
                    s = parts[:, i % 2]
                    pool.wait_ge(act_part, (j * TILES + i + 1) * NA)
                    pool.wait_ge(dve_part, (j * TILES + i + 1) * ND)
                    step = (j * TILES + i) * 4
                    for n, half in enumerate((8, 4, 2, 1)):
                        if n:
                            pool.wait_ge(pool_step, step + n)
                        pool.tensor_tensor(s[:, 0:half], s[:, 0:half], s[:, half:2 * half], ALU.add).then_inc(pool_step, 1)
                    pool.wait_ge(pool_step, step + 4)
                    if i == 0:
                        reach(pool, x2r_in[0], j * NBLK * 16)
                    if i == TILES // 2:
                        reach(pool, x2r_in[1], j * NBLK * 16)
                    pool.tensor_tensor(x2[:, i, :], s[:, 0, :], s[:, SUMS - 1, :], ALU.add).then_inc(x2_ready, 1)

            pool.wait_ge(v_prep, CHUNKS + 2)
            bodies(pool, body)

        @block.tensor
        def _(pe):
            def transpose_x0(n, q):
                reach(pe, z_ready, CHUNKS * n - 1)
                for r in range(TQ):
                    last = pe.transpose(sel_ps[(CHUNKS + 2) * q % 2][0:2 * F, r * P:(r + 1) * P],
                                        xs[:, q * TQ + r, :], ident[:])
                last.then_inc(xt_ready, 1)

            def select(n, q, i):
                if i == 0:
                    pe.wait_ge(xt_copied, n + 1)
                    reach(pe, z_ready, CHUNKS * n)
                elif i == 2:
                    pe.wait_ge(a_copied, n + 1)
                elif i > 2:
                    pe.wait_ge(z_ready, CHUNKS * n + i - 2)
                rows = RPC * F if i == 0 else rows_of(i - 1)
                pe.matmul(sel_ps[((CHUNKS + 2) * q + 1 + i) % 2][0:rows, :], sel[:, i, 0:rows], xt[:, :],
                          start=True, stop=True).then_inc(sel_ready, 1)

            def layer0(n, q, c):
                if c == 0:
                    reach(pe, x1_hi_ready, n)
                    reach(pe, x1_lo_ready, n)
                    reach(pe, s0_reduced, n)
                pe.wait_ge(z_hi_ready, CHUNKS * n + c + 1)
                pe.wait_ge(z_lo_ready, CHUNKS * n + c + 1)
                rows, k = rows_of(c), (CHUNKS * q + c) % 2
                terms = ((v_hi, z_hi), (v_lo, z_hi), (v_hi, z_lo))
                for i, (v, zz) in enumerate(terms):
                    last = pe.matmul(x1_ps[:], v[0:rows, c, :], zz[0:rows, k, :],
                                     start=(c == 0 and i == 0), stop=(c == CHUNKS - 1 and i == 2))
                last.then_inc(l0_done, 1)

            def layer1(j, i, u):
                q, r = divmod(i, TQ)
                if u == 0 and r == 0:
                    pe.wait_ge(x1_hi_ready, j * QUADS + q + 1)
                    pe.wait_ge(x1_lo_ready, j * QUADS + q + 1)
                pi, pu = (i, u - RING) if u >= RING else (i - 1, u - RING + BANKS)
                if pi >= 0 or has_prev(j):
                    act = pu in ACT_BANKS
                    reach(pe, act_part if act else dve_part,
                          (j * TILES + pi) * (NA if act else ND) + features_of(act, pu + 1))
                fs = bank_features(u)
                out = u_ps[(i * BANKS + u) % RING][:, 0:len(fs) * M]
                cols = slice(fs[0] * M, (fs[-1] + 1) * M)
                terms = ((x1_hi, w1_hi), (x1_hi, w1_lo), (x1_lo, w1_hi))
                for k, (x1, w) in enumerate(terms):
                    last = pe.matmul(out, x1[:, q % 2, r * P:(r + 1) * P], w[:, cols], start=(k == 0), stop=(k == 2))
                last.then_inc(u_ready, 1)

            def post(g, s):
                if s == DT_SLOT:
                    pe.wait_ge(dense_in, 16 * (g + 1))
                    reach(pe, y_copied, g)
                    pe.matmul(post_ps[0:DENSE, 384:512], dense_sb[:], ident[:], start=True, stop=True).then_inc(dt_ready, 1)
                if s in P2_SLOT:
                    t = P2_SLOT.index(s)
                    if t == 0:
                        pe.wait_ge(x2r_in[0], NBLK * 16 * (g + 1))
                        pe.wait_ge(x2r_in[1], NBLK * 16 * (g + 1))
                        pe.wait_ge(dt_copied, g + 1)
                    reach(pe, p2_copied, NBLK * g + t)
                    pe.wait_ge(blk_ready, (NBLK * g + t + 1) * BLK)
                    pe.matmul(post_ps[:, 0:BLK * FX], x2r[:, t, :], blk[:, t % 2].rearrange("p b f -> p (b f)"),
                              start=True, stop=True).then_inc(p2_ready, 1)
                first = (s - S2_SLOT) * S2_PER_SLOT
                if 0 <= first < F:
                    if first == 0:
                        pe.wait_ge(p2_copied, NBLK * (g + 1))
                    for f in range(first, min(F, first + S2_PER_SLOT)):
                        last = pe.matmul(post_ps[:, 0:P], w2_sb[:, f, :], p2[:, f, :], start=(f == 0), stop=(f == F - 1))
                    if f == F - 1:
                        last.then_inc(s2_ready, 1)
                if MLP1_SLOT <= s < MLP1_SLOT + H1 // P:
                    n = s - MLP1_SLOT
                    if n == 0:
                        pe.wait_ge(s2_copied, g + 1)
                        pe.wait_ge(s0_in_ready, g + 1)
                    for k, rhs in enumerate((s0_in[:], p2[:, F, :], s2_in[:], dense_t[:])):
                        last = pe.matmul(post_ps[:, n * P:(n + 1) * P], wt1_sb[:, k, n * P:(n + 1) * P], rhs,
                                         start=(k == 0), stop=(k == 3))
                    if n == H1 // P - 1:
                        last.then_inc(h1_ready, 1)
                if MLP2_SLOT <= s < MLP2_SLOT + H2 // P:
                    n = s - MLP2_SLOT
                    pe.wait_ge(h1_copied, (g + 1) * (H1 // P))
                    for k in range(H1 // P):
                        last = pe.matmul(post_ps[:, n * P:(n + 1) * P], wt2_sb[:, k, n * P:(n + 1) * P], h1[:, k, :],
                                         start=(k == 0), stop=(k == H1 // P - 1))
                    if n == H2 // P - 1:
                        last.then_inc(h2_ready, 1)
                if s == MLP3_SLOT:
                    pe.wait_ge(h2_copied, (g + 1) * (H2 // P))
                    for k in range(H2 // P):
                        last = pe.matmul(post_ps[0:1, 0:P], wt3_sb[:, k:k + 1], h2[:, k, :],
                                         start=(k == 0), stop=(k == H2 // P - 1))
                    last.then_inc(y_ready, 1)

            def ahead(n, q, at):
                if at == T_SLOT:
                    if q == 0:
                        pe.wait_ge(xs_hi, n // QUADS + 1 if isinstance(n, int) else group_of_next + 1)
                        pe.wait_ge(xs_lo, n // QUADS + 1 if isinstance(n, int) else group_of_next + 1)
                    transpose_x0(n, q)
                if at == A_SLOT:
                    select(n, q, 0)
                for c in range(CHUNKS):
                    if at == B_SLOT[c]:
                        select(n, q, 1 + c)
                    if at == B_SLOT[c] + 5:
                        layer0(n, q, c)

            def body(j):
                nonlocal group_of_next
                group_of_next = j + 1
                for s in range(SLOTS):
                    i, u = divmod(s, BANKS)
                    layer1(j, i, u)
                    nq = next_quad(j, s)
                    if nq:
                        ahead(*nq)
                    if has_prev(j):
                        post(j - 1, s)

            group_of_next = 0
            pe.wait_ge(consts_in, 16 * 3)
            pe.wait_ge(sel_cast, 1)
            for at in range(TQ * BANKS):
                if at == B_SLOT[0] + 5:
                    pe.wait_ge(v_hi_ready, 1)
                    pe.wait_ge(v_lo_ready, 1)
                ahead(0, 0, at)
            pe.wait_ge(w1_hi_ready, 1)
            pe.wait_ge(w1_lo_ready, 1)
            pe.wait_ge(w2_in, 16)
            pe.wait_ge(mlp_in, 16 * 6)
            bodies(pe, body)
            for s in range(SLOTS):
                post(GROUPS - 1, s)

        @block.scalar
        def _(act):
            act.dma_start(w1_stage, w1.rearrange("(f g) m -> g f m", g=M)).then_inc(w1_in, 16)

            def split_x0_hi(g):
                act.wait_ge(gathered, 16 * F * (g + 1))
                reach(act, xt_ready, QUADS * g)
                act.activation(xs[:, :, 0:F].bitcast(F32R), xg[:].rearrange("p (f d) -> p d f", d=D),
                               ACT.Copy).then_inc(xs_hi, 1)

            def ahead(n, q, at):
                if at == XT_SLOT:
                    act.wait_ge(xt_ready, n + 1)
                    reach(act, sel_ready, (1 + CHUNKS) * n)
                    act.activation(xt[:], sel_ps[(CHUNKS + 2) * q % 2][0:2 * F, :], ACT.Copy).then_inc(xt_copied, 1)
                if at == AC_SLOT:
                    act.wait_ge(sel_ready, (1 + CHUNKS) * n + 1)
                    reach(act, z_ready, CHUNKS * n)
                    act.activation(a_sb[:], sel_ps[((CHUNKS + 2) * q + 1) % 2][0:RPC * F, :],
                                   ACT.Copy).then_inc(a_copied, 1)
                for c in range(CHUNKS):
                    if at == B_SLOT[c] + 2:
                        rows, k = rows_of(c), (CHUNKS * q + c) % 2
                        act.wait_ge(z_ready, CHUNKS * n + c + 1)
                        reach(act, l0_done, CHUNKS * n + c - 1)
                        act.activation(z_hi[0:rows, k, :], z[0:rows, k, :], ACT.Copy).then_inc(z_hi_ready, 1)
                if at == X1H_SLOT:
                    act.wait_ge(l0_done, CHUNKS * (n + 1))
                    reach(act, u_ready, TQ * BANKS * (n - 1))
                    act.activation(x1_hi[:, q % 2, :], x1_ps[:], ACT.Copy).then_inc(x1_hi_ready, 1)

            def block_diagonal(g, t, part):
                if t == 0 and part == 0:
                    act.wait_ge(x0r_in, 2 * NBLK * 16 * (g + 1))
                if part == 0:
                    reach(act, p2_ready, NBLK * g + max(t - 1, 0))
                for b in range(BLK // 2 * part, BLK // 2 * (part + 1)):
                    act.activation(blk[:, t % 2, b, :], x0r[:, t, :], ACT.Copy, scale=mask[:, b:b + 1]).then_inc(blk_ready, 1)

            def post(g, s):
                if s == DT_SLOT + 1:
                    act.wait_ge(dt_ready, g + 1)
                    reach(act, h1_ready, g)
                    act.activation(dense_t[0:DENSE, :], post_ps[0:DENSE, 384:512], ACT.Copy).then_inc(dt_copied, 1)
                for t in range(NBLK):
                    if s == P2_SLOT[t] - 4:
                        block_diagonal(g, t, 0)
                    if s == P2_SLOT[t] - 2:
                        block_diagonal(g, t, 1)
                    if s == P2_SLOT[t] + 1:
                        act.wait_ge(p2_ready, NBLK * g + t + 1)
                        act.activation(p2[:, :, BLK * t:BLK * (t + 1)],
                                       post_ps[:, 0:BLK * FX].rearrange("p (b f) -> p f b", f=FX),
                                       ACT.Copy).then_inc(p2_copied, 1)
                if s == S2_SLOT + F // S2_PER_SLOT + 1:
                    act.wait_ge(s2_ready, g + 1)
                    act.activation(s2_in[:], post_ps[:, 0:P], ACT.Copy).then_inc(s2_copied, 1)
                if s == MLP1_SLOT + H1 // P:
                    act.wait_ge(h1_ready, g + 1)
                    for n in range(H1 // P):
                        act.activation(h1[:, n, :], post_ps[:, n * P:(n + 1) * P], ACT.Relu,
                                       bias=bt1_sb[:, n:n + 1]).then_inc(h1_copied, 1)
                if s == MLP2_SLOT + H2 // P:
                    act.wait_ge(h2_ready, g + 1)
                    for n in range(H2 // P):
                        act.activation(h2[:, n, :], post_ps[:, n * P:(n + 1) * P], ACT.Relu,
                                       bias=bt2_sb[:, n:n + 1]).then_inc(h2_copied, 1)
                if s == MLP3_SLOT + 1:
                    act.wait_ge(y_ready, g + 1)
                    reach(act, y_out, 16 * g)
                    act.activation(y_sb[:], post_ps[0:1, 0:P], ACT.Copy).then_inc(y_copied, 1)

            def body(j):
                act.wait_ge(gathered, 16 * F * (j + 1))
                reach(act, x0r_in, 2 * NBLK * 16 * j)
                reach(act, act_part, TILES * NA * j)
                act.activation(x_act[:, :, 0:F], xg[:].rearrange("p (f d) -> p d f", d=D), ACT.Copy).then_inc(x_act_ready, 1)
                act.wait_ge(x_act_ready, j + 1)
                for s in range(SLOTS):
                    i, u = divmod(s, BANKS)
                    if u in ACT_BANKS:
                        if u == ACT_BANKS[0]:
                            reach(act, x2_ready, j * TILES + i - 1)
                        act.wait_ge(u_ready, j * SLOTS + s + 1)
                        for k, f in enumerate(bank_features(u)):
                            act.activation(parts[:, i % 2, features_of(True, u) + k, :],
                                           u_ps[s % RING][:, k * M:(k + 1) * M], ACT.Copy,
                                           scale=x_act[:, i, f:f + 1]).then_inc(act_part, 1)
                    if s == XS_HI_SLOT and has_next(j):
                        split_x0_hi(j + 1)
                    nq = next_quad(j, s)
                    if nq:
                        ahead(*nq)
                    if has_prev(j):
                        post(j - 1, s)

            act.wait_ge(consts_in, 16 * 3)
            act.activation(sel[:].rearrange("p a b -> p (a b)"), sel_stage, ACT.Copy).then_inc(sel_cast, 1)
            act.wait_ge(w1_in, 16)
            act.activation(w1_hi[:], w1_stage, ACT.Copy).then_inc(w1_hi_ready, 1)
            act.wait_ge(v_prep, CHUNKS + 2)
            for c in range(CHUNKS):
                last = act.activation(v_hi[0:rows_of(c), c, :], vs[0:rows_of(c), c, :], ACT.Copy)
            last.then_inc(v_hi_ready, 1)
            split_x0_hi(0)
            act.wait_ge(zeroed, 3)
            for at in range(TQ * BANKS):
                ahead(0, 0, at)
            act.wait_ge(w1_lo_ready, 1)
            act.wait_ge(mlp_in, 16 * 6)
            act.wait_ge(sel_cast, 1)
            bodies(act, body)
            for s in range(SLOTS):
                post(GROUPS - 1, s)

        @block.vector
        def _(dve):
            def split_x0_lo(g):
                dve.wait_ge(xs_hi, g + 1)
                reach(dve, xt_ready, QUADS * g)
                dve.tensor_tensor(xs[:, :, F:2 * F].bitcast(F32R), xg[:].rearrange("p (f d) -> p d f", d=D), xs[:, :, 0:F],
                                  ALU.subtract).then_inc(xs_lo, 1)

            def ahead(n, q, at):
                for c in range(CHUNKS):
                    rows, k = rows_of(c), (CHUNKS * q + c) % 2
                    if at == B_SLOT[c] + 1:
                        if c == 0:
                            dve.wait_ge(a_copied, n + 1)
                        dve.wait_ge(sel_ready, (1 + CHUNKS) * n + c + 2)
                        reach(dve, z_hi_ready, CHUNKS * n + c - 1)
                        reach(dve, z_lo_ready, CHUNKS * n + c - 1)
                        dve.tensor_tensor(z[0:rows, k, :], a_sb[0:rows, :],
                                          sel_ps[((CHUNKS + 2) * q + 2 + c) % 2][0:rows, :], ALU.mult).then_inc(z_ready, 1)
                    if at == B_SLOT[c] + 3:
                        dve.wait_ge(z_hi_ready, CHUNKS * n + c + 1)
                        reach(dve, l0_done, CHUNKS * n + c - 1)
                        dve.tensor_tensor(z_lo[0:rows, k, :], z[0:rows, k, :], z_hi[0:rows, k, :].bitcast(FP32),
                                          ALU.subtract).then_inc(z_lo_ready, 1)
                if at == X1L_SLOT:
                    dve.wait_ge(x1_hi_ready, n + 1)
                    reach(dve, u_ready, TQ * BANKS * (n - 1))
                    dve.tensor_tensor(x1_lo[:, q % 2, :], x1_ps[:], x1_hi[:, q % 2, :].bitcast(FP32),
                                      ALU.subtract).then_inc(x1_lo_ready, 1)
                if at == S0_SLOT:
                    reach(dve, s0_added, n)
                    if q == 0:
                        reach(dve, s0_in_ready, group_next if not isinstance(n, int) else n // QUADS)
                    dve.tensor_reduce(s0_acc[:] if q == 0 else s0_quad[:], x1_ps[:].rearrange("m (d b) -> m b d", b=P),
                                      AX.X, ALU.add).then_inc(s0_reduced, 1)
                    dve.wait_ge(s0_reduced, n + 1)
                    if q == 0:
                        dve.nop().then_inc(s0_added, 1)
                    else:
                        dve.tensor_tensor(s0_acc[:], s0_acc[:], s0_quad[:], ALU.add).then_inc(s0_added, 1)

            def body(j):
                nonlocal group_next
                group_next = j + 1
                dve.wait_ge(gathered, 16 * F * (j + 1))
                reach(dve, dve_part, TILES * ND * j)
                dve.tensor_copy(x_dve[:], xg[:].rearrange("p (f d) -> p d f", d=D)).then_inc(x_dve_ready, 1)
                dve.wait_ge(x_dve_ready, j + 1)
                for s in range(SLOTS):
                    i, u = divmod(s, BANKS)
                    if u not in ACT_BANKS:
                        if u == 0:
                            reach(dve, x2_ready, j * TILES + i - 1)
                        dve.wait_ge(u_ready, j * SLOTS + s + 1)
                        for k, f in enumerate(bank_features(u)):
                            m = features_of(False, u) + k
                            acc = parts[:, i % 2, NA + m % 2, :]
                            prod = u_ps[s % RING][:, k * M:(k + 1) * M]
                            if m < 2:
                                dve.tensor_scalar(acc, prod, x_dve[:, i, f:f + 1], None, ALU.mult).then_inc(dve_part, 1)
                            else:
                                dve.wait_ge(dve_part, (j * TILES + i) * ND + m - 1)
                                dve.scalar_tensor_tensor(acc, prod, x_dve[:, i, f:f + 1], acc,
                                                         ALU.mult, ALU.add).then_inc(dve_part, 1)
                    if s == XS_LO_SLOT and has_next(j):
                        split_x0_lo(j + 1)
                    if s == S0_COPY_SLOT:
                        reach(dve, h1_ready, j)
                        dve.wait_ge(s0_added, (j + 1) * QUADS)
                        dve.tensor_copy(s0_in[:], s0_acc[:]).then_inc(s0_in_ready, 1)
                    nq = next_quad(j, s)
                    if nq:
                        ahead(*nq)

            dve.wait_ge(v_in, 16 * (4 * ROT - 2))
            for c in range(CHUNKS):
                dve.tensor_tensor(vs[0:rows_of(c), c, :], va[0:rows_of(c), c, :], vb[0:rows_of(c), c, :], ALU.add).then_inc(v_prep, 1)
            dve.wait_ge(v_prep, CHUNKS)
            dve.tensor_scalar(vs[0:F, 0, :], vs[0:F, 0, :], 0.5, None, ALU.mult).then_inc(v_prep, 1)
            dve.wait_ge(v_prep, CHUNKS + 1)
            dve.nop().then_inc(v_prep, 1)
            dve.wait_ge(v_hi_ready, 1)
            for c in range(CHUNKS):
                last = dve.tensor_tensor(v_lo[0:rows_of(c), c, :], vs[0:rows_of(c), c, :],
                                         v_hi[0:rows_of(c), c, :].bitcast(FP32), ALU.subtract)
            last.then_inc(v_lo_ready, 1)
            dve.wait_ge(w1_hi_ready, 1)
            dve.tensor_tensor(w1_lo[:], w1_stage, w1_hi[:].bitcast(FP32), ALU.subtract).then_inc(w1_lo_ready, 1)
            group_next = 0
            split_x0_lo(0)
            for at in range(TQ * BANKS):
                ahead(0, 0, at)
            bodies(dve, body)


def selection():
    s = np.zeros((2 * F, 1 + CHUNKS, RPC * F), np.float32)
    for i in range(1 + CHUNKS):
        for r in range(RPC):
            for f in range(F):
                g = f if i == 0 else (f + RPC * (i - 1) + r) % F
                s[g, i, F * r + f] = s[F + g, i, F * r + f] = 1.0
    return s.reshape(2 * F, -1)


def kernel(**inputs):
    import concourse.bacc as bacc
    from concourse.bass_utils import run_bass_kernel_spmd

    nc = bacc.Bacc("TRN2", target_bir_lowering=False, num_devices=1)
    arrays = {}

    def given(name, a):
        a = np.ascontiguousarray(a)
        arrays[name] = a
        return nc.dram_tensor(name, a.shape, mybir.dt.from_np(a.dtype), kind="ExternalInput").ap()

    ids = given("ids", inputs["ids"])
    dense = given("dense_ctx", inputs["dense_ctx"])
    tables = [given(f"tbl_{f}", inputs[f"tbl_{f}"]) for f in range(F)]
    w0, w1, w2 = (given(f"L0_rec_f{k}", inputs[f"L0_rec_f{k}"]) for k in range(3))
    wt1, bt1, wt2, bt2, wt3 = (given(k, inputs[k]) for k in ("W_top1", "b_top1", "W_top2", "b_top2", "W_top3"))
    c_ident = given("c_ident", np.eye(P, dtype=np.float32))
    c_sel = given("c_sel", selection())
    part = np.arange(P)
    c_mask = given("c_mask", ((part[:, None] // (D // 2)) % BLK == np.arange(BLK)[None, :]).astype(np.float32))
    y = nc.dram_tensor("y", (B, 1), FP32, kind="ExternalOutput").ap()
    build(nc, ids, dense, tables, w0, w1, w2, wt1, bt1, wt2, bt2, wt3, c_ident, c_sel, c_mask, y)
    r = run_bass_kernel_spmd(nc, [arrays], core_ids=[0])
    return r.results[0]["y"]
```

```python
import numpy as np
import concourse.bass as bass
from concourse import mybir
from concourse.alu_op_type import AluOpType as ALU
from contextlib import ExitStack

FP32 = mybir.dt.float32
F32R = mybir.dt.float32r
INT32 = mybir.dt.int32
ACT = mybir.ActivationFunctionType
AX = mybir.AxisListType

P = 128
B, F, D, M, DENSE = 1024, 39, 16, 128, 16
H1, H2 = 512, 256
GROUPS = B // P
TILES = D
TQ = 4
QUADS = TILES // TQ
COLS = TQ * P
ROT = F // 2 + 1
RPC = 3
CHUNKS = -(-ROT // RPC)
FPB = 4
BANKS = -(-F // FPB)
RING = 4
SLOTS = TILES * BANKS
ACT_BANKS = ((1, 4, 6, 9), (1, 3, 5, 7, 9))
BLK = 8
NBLK = P // BLK
BLK_RING = 4
NARR = 8
FX = F + 1


def bank_features(u):
    return range(FPB * u, min(F, FPB * u + FPB))


def features_of(act, i, u=BANKS):
    return sum(len(bank_features(k)) for k in range(u) if (k in ACT_BANKS[i % 2]) == act)


def features_before(act, i, u=0):
    return sum(features_of(act, k) for k in range(i)) + (features_of(act, i, u) if u else 0)


NA, ND = features_before(True, TILES), features_before(False, TILES)
SUMS = max(features_of(True, i) for i in range(2)) + 2


def halvings(n):
    steps, left = [], []
    while n > 1:
        steps.append((0, n // 2, n // 2))
        if n % 2:
            left.append(n - 1)
        n //= 2
    while len(left) > 1:
        steps.append((0, left.pop(), 1))
    return steps if left else steps[:-1], (left or [1])[0]


def steps_before(i):
    return sum(len(halvings(features_of(True, k) + 2)[0]) for k in range(i))


QSLOTS = TQ * BANKS
T_AT, XT_AT, A_AT, AC_AT = -20, -18, -14, -13
B_AT = [-13 + 5 * c for c in range(CHUNKS)]
Z_AT = [at + 2 for at in B_AT]
HI_AT = [at + 4 for at in B_AT]
LO_AT = [at + 6 for at in B_AT]
L0_AT = [at + 11 for at in B_AT]
X1H_AT, X1L_AT, S0_AT = L0_AT[-1] + 1, L0_AT[-1] + 3, L0_AT[-1] + 6
DT_SLOT = 18
P2_SLOT = [27 + 4 * t for t in range(NBLK)]
BLK_AHEAD = 4
S2_SLOT, S2_PER_SLOT = 114, 2
MLP1_SLOT, MLP2_SLOT, MLP3_SLOT = 140, 148, 154
S0_COPY_SLOT = 149
XS_HI_SLOT, XS_LO_SLOT = 95, 97
GATHER_TILE, GATHER_TILES = 10, 15


def rows_of(c):
    return F * min(RPC, ROT - RPC * c)


def build(nc, ids, dense, tables, w0, w1, w2, wt1, bt1, wt2, bt2, wt3, c_ident, c_sel, c_mask, y):
    ctx = ExitStack()
    with ctx:
        def sb(name, shape, dt=FP32):
            return ctx.enter_context(nc.sbuf_tensor(name, shape, dt))

        def pb(name, shape):
            return ctx.enter_context(nc.psum_tensor(name, shape, FP32))

        def sem(name):
            return ctx.enter_context(nc.semaphore(name))

        ident = sb("ident", [P, P])
        sel = sb("sel", [2 * F, 1 + CHUNKS, RPC * F], F32R)
        mask = sb("mask", [P, BLK])
        v_hi = sb("v_hi", [RPC * F, CHUNKS, M], F32R)
        v_lo = sb("v_lo", [RPC * F, CHUNKS, M], F32R)
        w1_hi = sb("w1_hi", [M, F * M], F32R)
        w1_lo = sb("w1_lo", [M, F * M], F32R)
        w2_sb = sb("w2_sb", [M, F, M])
        wt1_sb = sb("wt1_sb", [P, 4, H1])
        wt2_sb = sb("wt2_sb", [P, H1 // P, H2])
        wt3_sb = sb("wt3_sb", [P, H2 // P])
        bt1_sb = sb("bt1_sb", [P, H1 // P])
        bt2_sb = sb("bt2_sb", [P, H2 // P])
        ids_all = sb("ids_all", [P, GROUPS, F], INT32)
        ids_sb = sb("ids_sb", [P, F], INT32)
        xg = sb("xg", [P, F * D])
        x_next = sb("x_next", [P, D, F])
        x_dve = sb("x_dve", [P, D, F])
        x_act = sb("x_act", [P, D, FX])
        xs = sb("xs", [P, D, 2 * F])
        xt = sb("xt", [2 * F, COLS], F32R)
        a_sb = sb("a_sb", [RPC * F, COLS])
        z = sb("z", [RPC * F, 2, COLS])
        z_hi = sb("z_hi", [RPC * F, 2, COLS], F32R)
        z_lo = sb("z_lo", [RPC * F, 2, COLS], F32R)
        x1_hi = sb("x1_hi", [M, 2, COLS], F32R)
        x1_lo = sb("x1_lo", [M, 2, COLS], F32R)
        parts = sb("parts", [P, 2, SUMS, M])
        x2 = sb("x2", [P, D, M])
        x2r = sb("x2r", [P, NBLK, M])
        x0r = sb("x0r", [P, NBLK, FX])
        blk = sb("blk", [P, BLK_RING, BLK, FX])
        p2 = sb("p2", [M, FX, P])
        s0_acc = sb("s0_acc", [M, P])
        s0_quad = sb("s0_quad", [M, P])
        s0_in = sb("s0_in", [M, P])
        s2_in = sb("s2_in", [M, P])
        dense_sb = sb("dense_sb", [P, DENSE])
        dense_t = sb("dense_t", [P, P])
        h1 = sb("h1", [P, H1 // P, P])
        h2 = sb("h2", [P, H2 // P, P])
        y_sb = sb("y_sb", [1, P])
        w1_stage = p2[:, 0:F, :].rearrange("g f m -> g (f m)")
        va, vb, vs = x2[0:RPC * F, 0:CHUNKS, :], x2[0:RPC * F, CHUNKS:2 * CHUNKS, :], x2r[0:RPC * F, 0:CHUNKS, :]
        sel_stage = parts[0:2 * F, 0, 0:8, :].rearrange("p a b -> p (a b)")[:, 0:(1 + CHUNKS) * RPC * F]

        w0_twice = nc.dram_tensor("w0_twice", (2, F, 2 * F, M), FP32).ap()

        u_ps = [pb(f"u_ps{i}", [P, FPB * M]) for i in range(RING)]
        sel_ps = [pb(f"sel_ps{i}", [P, COLS]) for i in range(2)]
        x1_ps = pb("x1_ps", [M, COLS])
        post_ps = pb("post_ps", [P, 512])

        consts_in = sem("consts_in")
        w0_in = sem("w0_in")
        v_in = sem("v_in")
        w1_in = sem("w1_in")
        w2_in = sem("w2_in")
        mlp_in = sem("mlp_in")
        ids_in = sem("ids_in")
        ids_ready = sem("ids_ready")
        passed = {"sp": sem("sp_passed"), "pool": sem("pool_passed")}
        dense_in = sem("dense_in")
        gathered = sem("gathered")
        x0r_in = sem("x0r_in")
        x2r_in0 = [sem("x2r_in0")]
        x2r_in1 = [sem(f"x2r_in1_{n}") for n in range(NARR)]
        y_out = sem("y_out")
        zeroed = sem("zeroed")
        v_prep = sem("v_prep")
        v_hi_ready = sem("v_hi_ready")
        v_lo_ready = sem("v_lo_ready")
        sel_cast = sem("sel_cast")
        w1_hi_ready = sem("w1_hi_ready")
        w1_lo_ready = sem("w1_lo_ready")
        x_next_ready = sem("x_next_ready")
        xs_hi = sem("xs_hi")
        xs_lo = sem("xs_lo")
        x_act_ready = sem("x_act_ready")
        x_dve_ready = sem("x_dve_ready")
        xt_ready = sem("xt_ready")
        xt_copied = sem("xt_copied")
        sel_ready = sem("sel_ready")
        a_copied = sem("a_copied")
        z_ready = sem("z_ready")
        z_hi_ready = sem("z_hi_ready")
        z_lo_ready = sem("z_lo_ready")
        l0_done = sem("l0_done")
        x1_hi_ready = sem("x1_hi_ready")
        x1_lo_ready = sem("x1_lo_ready")
        s0_reduced = sem("s0_reduced")
        s0_added = sem("s0_added")
        s0_in_ready = sem("s0_in_ready")
        u_ready = sem("u_ready")
        act_part = sem("act_part")
        dve_part = sem("dve_part")
        add_step = sem("add_step")
        x2_ready = sem("x2_ready")
        blk_ready = sem("blk_ready")
        p2_ready = sem("p2_ready")
        p2_copied = sem("p2_copied")
        s2_ready = sem("s2_ready")
        s2_copied = sem("s2_copied")
        dt_ready = sem("dt_ready")
        dt_copied = sem("dt_copied")
        h1_ready = sem("h1_ready")
        h1_copied = sem("h1_copied")
        h2_ready = sem("h2_ready")
        h2_copied = sem("h2_copied")
        y_ready = sem("y_ready")
        y_copied = sem("y_copied")

        block = ctx.enter_context(nc.Block())

        def reach(eng, s, value):
            if not isinstance(value, int) or value > 0:
                eng.wait_ge(s, value)

        def bodies(eng, body):
            body(0)
            with eng.Fori(1, GROUPS - 2) as j:
                body(j)
            body(GROUPS - 2)
            body(GROUPS - 1)

        def has_prev(j):
            return not (isinstance(j, int) and j == 0)

        def has_next(j):
            return not (isinstance(j, int) and j == GROUPS - 1)

        def has_next2(j):
            return not (isinstance(j, int) and j >= GROUPS - 2)

        def due(j, s, at):
            if (s - at) % QSLOTS:
                return None
            m = (s - at) // QSLOTS + 1
            if m < 0 or (m >= QUADS and not has_next(j)):
                return None
            return j * QUADS + m, m % QUADS, j + m // QUADS

        def chunk_due(j, s, ats):
            for c, at in enumerate(ats):
                if due(j, s, at):
                    return (c, *due(j, s, at))
            return None

        def before_body0():
            return range(T_AT - QSLOTS, 0)

        def by_vector(j, i):
            return isinstance(j, int) and j == GROUPS - 1 and i == TILES - 1

        def add_up(eng, j, i):
            s = parts[:, i % 2]
            eng.wait_ge(act_part, j * NA + features_before(True, i + 1))
            eng.wait_ge(dve_part, j * ND + features_before(False, i + 1))
            steps, left = halvings(features_of(True, i) + 2)
            done = j * steps_before(TILES) + steps_before(i)
            for n, (to, of, count) in enumerate(steps):
                if n:
                    eng.wait_ge(add_step, done + n)
                eng.tensor_tensor(s[:, to:to + count], s[:, to:to + count], s[:, of:of + count],
                                  ALU.add).then_inc(add_step, 1)
            eng.wait_ge(add_step, done + len(steps))
            if i == 0:
                reach(eng, x2r_in0[0], j * NBLK * 16)
            if i == TILES // 2:
                for arrived in x2r_in1:
                    reach(eng, arrived, j * NBLK // NARR * 16)
            eng.tensor_tensor(x2[:, i, :], s[:, 0, :], s[:, left, :], ALU.add).then_inc(x2_ready, 1)

        @block.sync
        def _(sp):
            sp.dma_start(ids_all[:], ids.rearrange("(j p) f -> p j f", p=P)).then_inc(ids_in, 16)
            sp.dma_start(ident[:], c_ident).then_inc(consts_in, 16)
            sp.dma_start(mask[:], c_mask).then_inc(consts_in, 16)
            sp.dma_start(sel_stage, c_sel).then_inc(consts_in, 16)
            for mirrored in range(2):
                src = w0.rearrange("(g f) m -> f g m" if mirrored else "(f g) m -> f g m", g=F)
                for twice in range(2):
                    sp.dma_start(w0_twice[mirrored, :, F * twice:F * (twice + 1), :], src).then_inc(w0_in, 16)
            sp.wait_ge(w0_in, 16 * 4)
            for mirrored, dst in ((0, va), (1, vb)):
                for r in range(RPC):
                    n = len(range(r, ROT, RPC))
                    flat = w0_twice[mirrored].rearrange("f g m -> (f g) m")
                    rows = bass.AP(tensor=flat.tensor, offset=flat.offset + r * M,
                                   ap=[[(2 * F + 1) * M, F], [RPC * M, n], [1, M]])
                    sp.dma_start(dst[F * r:F * (r + 1), 0:n, :], rows).then_inc(v_in, 16)
            sp.dma_start(w2_sb[:], w2.rearrange("(f g) m -> g f m", g=M)).then_inc(w2_in, 16)
            sp.wait_ge(zeroed, 3)
            sp.dma_start(wt1_sb[:, 0:3, :], wt1[0:3 * P, :].rearrange("(k p) n -> p k n", p=P)).then_inc(mlp_in, 16)
            sp.dma_start(wt1_sb[0:DENSE, 3, :], wt1[3 * P:3 * P + DENSE, :]).then_inc(mlp_in, 16)
            sp.dma_start(wt2_sb[:], wt2.rearrange("(k p) n -> p k n", p=P)).then_inc(mlp_in, 16)
            with nc.allow_non_contiguous_dma(reason="biases and the last layer's column, once"):
                sp.dma_start(wt3_sb[:], wt3.rearrange("(k p) n -> p (k n)", p=P)).then_inc(mlp_in, 16)
                sp.dma_start(bt1_sb[:], bt1.rearrange("(k p) -> p k", p=P)).then_inc(mlp_in, 16)
                sp.dma_start(bt2_sb[:], bt2.rearrange("(k p) -> p k", p=P)).then_inc(mlp_in, 16)

            def regroup(half, dst, src, arrived):
                rows = BLK * D // 2
                for t in range(NBLK):
                    sp.dma_start(dst[half * rows:(half + 1) * rows, t, :],
                                 src[BLK * t:BLK * (t + 1), half * D // 2:(half + 1) * D // 2, :]
                                 ).then_inc(arrived[t * len(arrived) // NBLK], 16)

            def sp_wait(semaphore, value):
                if not isinstance(value, int) or value > 0:
                    sp.wait_ge(semaphore, value)
                    sp.sem_inc(passed["sp"], 1)

            def body(j):
                sp_wait(x_act_ready, j + 1)
                sp_wait(blk_ready, j * NBLK)
                for half in range(2):
                    regroup(half, x0r, x_act, [x0r_in])
                sp_wait(p2_ready, j * NBLK)
                sp_wait(x2_ready, j * TILES + TILES // 2)
                regroup(0, x2r, x2, x2r_in0)
                if has_prev(j):
                    store_y(j - 1)
                    sp_wait(y_out, 16 * j)
                sp_wait(dt_ready, j)
                sp.dma_start(dense_sb[:], dense[bass.ts(j, P), :]).then_inc(dense_in, 16)
                sp_wait(x2_ready, (j + 1) * TILES)
                regroup(1, x2r, x2, x2r_in1)

            def store_y(g):
                sp_wait(y_copied, g + 1)
                sp.dma_start(y[bass.ts(g, P), :].rearrange("b n -> n b"), y_sb[:]).then_inc(y_out, 16)

            bodies(sp, body)
            store_y(GROUPS - 1)
            sp.wait_ge(y_out, 16 * GROUPS)

        @block.gpsimd
        def _(pool):
            pool.memset(x_act[:], 1.0).then_inc(zeroed, 1)
            pool.memset(dense_t[:], 0.0).then_inc(zeroed, 1)
            pool.memset(wt1_sb[:, 3, :], 0.0).then_inc(zeroed, 1)

            def gather(f):
                pool.indirect_dma_start(xg[:, D * f:D * (f + 1)], None, tables[f],
                                        bass.IndirectOffsetOnAxis(ap=ids_sb[:, f:f + 1], axis=0)).then_inc(gathered, 16)

            def take_ids(g):
                reach(pool, gathered, 16 * F * g)
                src = ids_all[:, g, :] if isinstance(g, int) else ids_all[:, bass.ds(g, 1), :].rearrange("p a f -> p (a f)")
                pool.tensor_copy(ids_sb[:], src).then_inc(ids_ready, 1)
                pool.wait_ge(ids_ready, g + 1)
                pool.sem_inc(passed["pool"], 1)

            def gathers(g, first, last):
                if first == 0:
                    reach(pool, x_next_ready, g)
                    reach(pool, xs_hi, g)
                    reach(pool, xs_lo, g)
                    take_ids(g)
                for f in range(first, last):
                    gather(f)

            def spread(n):
                return min(F, -(-F * n // GATHER_TILES))

            pool.wait_ge(ids_in, 16)
            gathers(0, 0, F)
            gathers(1, 0, spread(TILES - GATHER_TILE))

            def body(j):
                for i in range(TILES):
                    if i < GATHER_TILE and has_next(j):
                        n = i + TILES - GATHER_TILE
                        gathers(j + 1, spread(n), spread(n + 1))
                    if i >= GATHER_TILE and has_next2(j):
                        n = i - GATHER_TILE
                        gathers(j + 2, spread(n), spread(n + 1))
                    if not by_vector(j, i):
                        add_up(pool, j, i)

            pool.wait_ge(v_prep, CHUNKS + 2)
            bodies(pool, body)

        @block.tensor
        def _(pe):
            def transpose_x0(n, q, g):
                if q == 0:
                    pe.wait_ge(xs_hi, g + 1)
                    pe.wait_ge(xs_lo, g + 1)
                reach(pe, z_ready, CHUNKS * n - 1)
                for r in range(TQ):
                    last = pe.transpose(sel_ps[(CHUNKS + 2) * q % 2][0:2 * F, r * P:(r + 1) * P],
                                        xs[:, q * TQ + r, :], ident[:])
                last.then_inc(xt_ready, 1)

            def select(n, q, i):
                if i == 0:
                    pe.wait_ge(xt_copied, n + 1)
                    reach(pe, z_ready, CHUNKS * n)
                elif i == 2:
                    pe.wait_ge(a_copied, n + 1)
                elif i > 2:
                    pe.wait_ge(z_ready, CHUNKS * n + i - 2)
                rows = RPC * F if i == 0 else rows_of(i - 1)
                pe.matmul(sel_ps[((CHUNKS + 2) * q + 1 + i) % 2][0:rows, :], sel[:, i, 0:rows], xt[:, :],
                          start=True, stop=True).then_inc(sel_ready, 1)

            def layer0(n, q, c):
                if c == 0:
                    reach(pe, x1_hi_ready, n)
                    reach(pe, x1_lo_ready, n)
                    reach(pe, s0_reduced, n)
                pe.wait_ge(z_hi_ready, CHUNKS * n + c + 1)
                pe.wait_ge(z_lo_ready, CHUNKS * n + c + 1)
                rows, k = rows_of(c), (CHUNKS * q + c) % 2
                terms = ((v_hi, z_hi), (v_lo, z_hi), (v_hi, z_lo))
                for i, (v, zz) in enumerate(terms):
                    last = pe.matmul(x1_ps[:], v[0:rows, c, :], zz[0:rows, k, :],
                                     start=(c == 0 and i == 0), stop=(c == CHUNKS - 1 and i == 2))
                last.then_inc(l0_done, 1)

            def layer1(j, i, u):
                q, r = divmod(i, TQ)
                if u == 0 and r == 0:
                    pe.wait_ge(x1_hi_ready, j * QUADS + q + 1)
                    pe.wait_ge(x1_lo_ready, j * QUADS + q + 1)
                pi, pu = (i, u - RING) if u >= RING else (i - 1, u - RING + BANKS)
                if pi >= 0 or has_prev(j):
                    act = pu in ACT_BANKS[pi % 2]
                    taken = features_before(act, pi, pu + 1) if pi >= 0 else \
                        features_before(act, TILES - 1, pu + 1) - (NA if act else ND)
                    reach(pe, act_part if act else dve_part, j * (NA if act else ND) + taken)
                fs = bank_features(u)
                out = u_ps[(i * BANKS + u) % RING][:, 0:len(fs) * M]
                cols = slice(fs[0] * M, (fs[-1] + 1) * M)
                terms = ((x1_hi, w1_hi), (x1_hi, w1_lo), (x1_lo, w1_hi))
                for k, (x1, w) in enumerate(terms):
                    last = pe.matmul(out, x1[:, q % 2, r * P:(r + 1) * P], w[:, cols], start=(k == 0), stop=(k == 2))
                last.then_inc(u_ready, 1)

            def post(g, s, banks=(post_ps,)):
                if s == DT_SLOT:
                    pe.wait_ge(dense_in, 16 * (g + 1))
                    pe.matmul(post_ps[0:DENSE, 384:512], dense_sb[:], ident[:], start=True, stop=True).then_inc(dt_ready, 1)
                if s in P2_SLOT:
                    t = P2_SLOT.index(s)
                    if t == 0:
                        pe.wait_ge(x2r_in0[0], NBLK * 16 * (g + 1))
                        pe.wait_ge(dt_copied, g + 1)
                    if t % (NBLK // NARR) == 0:
                        pe.wait_ge(x2r_in1[t * NARR // NBLK], NBLK // NARR * 16 * (g + 1))
                    if t >= len(banks):
                        pe.wait_ge(p2_copied, NBLK * g + t + 1 - len(banks))
                    pe.wait_ge(blk_ready, NBLK * g + t + 1)
                    pe.matmul(banks[t % len(banks)][:, 0:BLK * FX], x2r[:, t, :], blk[:, t % BLK_RING].rearrange("p b f -> p (b f)"),
                              start=True, stop=True).then_inc(p2_ready, 1)
                first = (s - S2_SLOT) * S2_PER_SLOT
                if 0 <= first < F:
                    if first == 0:
                        pe.wait_ge(p2_copied, NBLK * (g + 1))
                    for f in range(first, min(F, first + S2_PER_SLOT)):
                        last = pe.matmul(post_ps[:, 0:P], w2_sb[:, f, :], p2[:, f, :], start=(f == 0), stop=(f == F - 1))
                    if f == F - 1:
                        last.then_inc(s2_ready, 1)
                if MLP1_SLOT <= s < MLP1_SLOT + H1 // P:
                    n = s - MLP1_SLOT
                    if n == 0:
                        pe.wait_ge(s2_copied, g + 1)
                        pe.wait_ge(s0_in_ready, g + 1)
                    for k, rhs in enumerate((s0_in[:], p2[:, F, :], s2_in[:], dense_t[:])):
                        last = pe.matmul(post_ps[:, n * P:(n + 1) * P], wt1_sb[:, k, n * P:(n + 1) * P], rhs,
                                         start=(k == 0), stop=(k == 3))
                    if n == H1 // P - 1:
                        last.then_inc(h1_ready, 1)
                if MLP2_SLOT <= s < MLP2_SLOT + H2 // P:
                    n = s - MLP2_SLOT
                    pe.wait_ge(h1_copied, (g + 1) * (H1 // P))
                    for k in range(H1 // P):
                        last = pe.matmul(post_ps[:, n * P:(n + 1) * P], wt2_sb[:, k, n * P:(n + 1) * P], h1[:, k, :],
                                         start=(k == 0), stop=(k == H1 // P - 1))
                    if n == H2 // P - 1:
                        last.then_inc(h2_ready, 1)
                if s == MLP3_SLOT:
                    pe.wait_ge(h2_copied, (g + 1) * (H2 // P))
                    for k in range(H2 // P):
                        last = pe.matmul(post_ps[0:1, 0:P], wt3_sb[:, k:k + 1], h2[:, k, :],
                                         start=(k == 0), stop=(k == H2 // P - 1))
                    last.then_inc(y_ready, 1)

            def ahead(j, s):
                if due(j, s, T_AT):
                    transpose_x0(*due(j, s, T_AT))
                if due(j, s, A_AT):
                    n, q, _ = due(j, s, A_AT)
                    select(n, q, 0)
                if chunk_due(j, s, B_AT):
                    c, n, q, _ = chunk_due(j, s, B_AT)
                    select(n, q, 1 + c)
                if chunk_due(j, s, L0_AT):
                    c, n, q, _ = chunk_due(j, s, L0_AT)
                    layer0(n, q, c)

            def body(j):
                for s in range(SLOTS):
                    i, u = divmod(s, BANKS)
                    layer1(j, i, u)
                    ahead(j, s)
                    if has_prev(j):
                        post(j - 1, s)

            pe.wait_ge(consts_in, 16 * 3)
            pe.wait_ge(sel_cast, 1)
            for s in before_body0():
                if s == L0_AT[0] - QSLOTS:
                    pe.wait_ge(v_hi_ready, 1)
                    pe.wait_ge(v_lo_ready, 1)
                ahead(0, s)
            pe.wait_ge(w1_hi_ready, 1)
            pe.wait_ge(w1_lo_ready, 1)
            pe.wait_ge(w2_in, 16)
            pe.wait_ge(mlp_in, 16 * 6)
            bodies(pe, body)
            pe.wait_ge(dve_part, GROUPS * ND)
            pe.wait_ge(act_part, GROUPS * NA)
            for s in range(SLOTS):
                post(GROUPS - 1, s, (post_ps, *u_ps[0:3]))

        @block.scalar
        def _(act):
            act.dma_start(w1_stage, w1.rearrange("(f g) m -> g f m", g=M)).then_inc(w1_in, 16)

            def split_x0_hi(g):
                act.wait_ge(gathered, 16 * F * (g + 1))
                reach(act, xt_ready, QUADS * g)
                reach(act, x_act_ready, g)
                reach(act, x_dve_ready, g)
                act.activation(xs[:, :, 0:F].bitcast(F32R), xg[:].rearrange("p (f d) -> p d f", d=D),
                               ACT.Copy).then_inc(xs_hi, 1)
                act.activation(x_next[:], xg[:].rearrange("p (f d) -> p d f", d=D), ACT.Copy).then_inc(x_next_ready, 1)

            def ahead(j, s):
                if due(j, s, XT_AT):
                    n, q, _ = due(j, s, XT_AT)
                    act.wait_ge(xt_ready, n + 1)
                    reach(act, sel_ready, (1 + CHUNKS) * n)
                    act.activation(xt[:], sel_ps[(CHUNKS + 2) * q % 2][0:2 * F, :], ACT.Copy).then_inc(xt_copied, 1)
                if due(j, s, AC_AT):
                    n, q, _ = due(j, s, AC_AT)
                    act.wait_ge(sel_ready, (1 + CHUNKS) * n + 1)
                    reach(act, z_ready, CHUNKS * n)
                    act.activation(a_sb[:], sel_ps[((CHUNKS + 2) * q + 1) % 2][0:RPC * F, :],
                                   ACT.Copy).then_inc(a_copied, 1)
                if chunk_due(j, s, HI_AT):
                    c, n, q, _ = chunk_due(j, s, HI_AT)
                    rows, k = rows_of(c), (CHUNKS * q + c) % 2
                    act.wait_ge(z_ready, CHUNKS * n + c + 1)
                    reach(act, l0_done, CHUNKS * n + c - 1)
                    act.activation(z_hi[0:rows, k, :], z[0:rows, k, :], ACT.Copy).then_inc(z_hi_ready, 1)
                if due(j, s, X1H_AT):
                    n, q, _ = due(j, s, X1H_AT)
                    act.wait_ge(l0_done, CHUNKS * (n + 1))
                    reach(act, u_ready, QSLOTS * (n - 1))
                    act.activation(x1_hi[:, q % 2, :], x1_ps[:], ACT.Copy).then_inc(x1_hi_ready, 1)

            def post(g, s, banks=(post_ps,)):
                if s == DT_SLOT + 1:
                    act.wait_ge(dt_ready, g + 1)
                    act.activation(dense_t[0:DENSE, :], post_ps[0:DENSE, 384:512], ACT.Copy).then_inc(dt_copied, 1)
                for t in range(NBLK):
                    if s == P2_SLOT[t] + 1:
                        act.wait_ge(p2_ready, NBLK * g + t + 1)
                        act.activation(p2[:, :, BLK * t:BLK * (t + 1)],
                                       banks[t % len(banks)][:, 0:BLK * FX].rearrange("p (b f) -> p f b", f=FX),
                                       ACT.Copy).then_inc(p2_copied, 1)
                if s == S2_SLOT + F // S2_PER_SLOT + 1:
                    act.wait_ge(s2_ready, g + 1)
                    act.activation(s2_in[:], post_ps[:, 0:P], ACT.Copy).then_inc(s2_copied, 1)
                if s == MLP1_SLOT + H1 // P:
                    act.wait_ge(h1_ready, g + 1)
                    for n in range(H1 // P):
                        act.activation(h1[:, n, :], post_ps[:, n * P:(n + 1) * P], ACT.Relu,
                                       bias=bt1_sb[:, n:n + 1]).then_inc(h1_copied, 1)
                if s == MLP2_SLOT + H2 // P:
                    act.wait_ge(h2_ready, g + 1)
                    for n in range(H2 // P):
                        act.activation(h2[:, n, :], post_ps[:, n * P:(n + 1) * P], ACT.Relu,
                                       bias=bt2_sb[:, n:n + 1]).then_inc(h2_copied, 1)
                if s == MLP3_SLOT + 1:
                    act.wait_ge(y_ready, g + 1)
                    act.activation(y_sb[:], post_ps[0:1, 0:P], ACT.Copy).then_inc(y_copied, 1)

            def body(j):
                act.wait_ge(x_next_ready, j + 1)
                reach(act, x0r_in, 2 * NBLK * 16 * j)
                reach(act, act_part, NA * j)
                act.activation(x_act[:, :, 0:F], x_next[:], ACT.Copy).then_inc(x_act_ready, 1)
                act.wait_ge(x_act_ready, j + 1)
                for s in range(SLOTS):
                    i, u = divmod(s, BANKS)
                    if u in ACT_BANKS[i % 2]:
                        if u == ACT_BANKS[i % 2][0]:
                            reach(act, x2_ready, j * TILES + i - 1)
                        act.wait_ge(u_ready, j * SLOTS + s + 1)
                        for k, f in enumerate(bank_features(u)):
                            act.activation(parts[:, i % 2, features_of(True, i, u) + k, :],
                                           u_ps[s % RING][:, k * M:(k + 1) * M], ACT.Copy,
                                           scale=x_act[:, i, f:f + 1]).then_inc(act_part, 1)
                    if s == XS_HI_SLOT and has_next(j):
                        split_x0_hi(j + 1)
                    ahead(j, s)
                    if has_prev(j):
                        post(j - 1, s)

            act.wait_ge(consts_in, 16 * 3)
            act.activation(sel[:].rearrange("p a b -> p (a b)"), sel_stage, ACT.Copy).then_inc(sel_cast, 1)
            act.wait_ge(w1_in, 16)
            act.activation(w1_hi[:], w1_stage, ACT.Copy).then_inc(w1_hi_ready, 1)
            act.wait_ge(v_prep, CHUNKS + 2)
            for c in range(CHUNKS):
                last = act.activation(v_hi[0:rows_of(c), c, :], vs[0:rows_of(c), c, :], ACT.Copy)
            last.then_inc(v_hi_ready, 1)
            split_x0_hi(0)
            act.wait_ge(zeroed, 3)
            for s in before_body0():
                ahead(0, s)
            act.wait_ge(w1_lo_ready, 1)
            act.wait_ge(mlp_in, 16 * 6)
            act.wait_ge(sel_cast, 1)
            bodies(act, body)
            for s in range(SLOTS):
                post(GROUPS - 1, s, (post_ps, *u_ps[0:3]))

        @block.vector
        def _(dve):
            def split_x0_lo(g):
                dve.wait_ge(xs_hi, g + 1)
                reach(dve, xt_ready, QUADS * g)
                dve.tensor_tensor(xs[:, :, F:2 * F].bitcast(F32R), xg[:].rearrange("p (f d) -> p d f", d=D), xs[:, :, 0:F],
                                  ALU.subtract).then_inc(xs_lo, 1)

            def ahead(j, s):
                if chunk_due(j, s, Z_AT):
                    c, n, q, _ = chunk_due(j, s, Z_AT)
                    rows, k = rows_of(c), (CHUNKS * q + c) % 2
                    if c == 0:
                        dve.wait_ge(a_copied, n + 1)
                    dve.wait_ge(sel_ready, (1 + CHUNKS) * n + c + 2)
                    reach(dve, z_hi_ready, CHUNKS * n + c - 1)
                    reach(dve, z_lo_ready, CHUNKS * n + c - 1)
                    dve.tensor_tensor(z[0:rows, k, :], a_sb[0:rows, :],
                                      sel_ps[((CHUNKS + 2) * q + 2 + c) % 2][0:rows, :], ALU.mult).then_inc(z_ready, 1)
                if chunk_due(j, s, LO_AT):
                    c, n, q, _ = chunk_due(j, s, LO_AT)
                    rows, k = rows_of(c), (CHUNKS * q + c) % 2
                    dve.wait_ge(z_hi_ready, CHUNKS * n + c + 1)
                    reach(dve, l0_done, CHUNKS * n + c - 1)
                    dve.tensor_tensor(z_lo[0:rows, k, :], z[0:rows, k, :], z_hi[0:rows, k, :].bitcast(FP32),
                                      ALU.subtract).then_inc(z_lo_ready, 1)
                if due(j, s, X1L_AT):
                    n, q, _ = due(j, s, X1L_AT)
                    dve.wait_ge(x1_hi_ready, n + 1)
                    reach(dve, u_ready, QSLOTS * (n - 1))
                    dve.tensor_tensor(x1_lo[:, q % 2, :], x1_ps[:], x1_hi[:, q % 2, :].bitcast(FP32),
                                      ALU.subtract).then_inc(x1_lo_ready, 1)
                if due(j, s, S0_AT):
                    n, q, g = due(j, s, S0_AT)
                    reach(dve, s0_added, n)
                    if q == 0:
                        reach(dve, s0_in_ready, g)
                    dve.tensor_reduce(s0_acc[:] if q == 0 else s0_quad[:], x1_ps[:].rearrange("m (d b) -> m b d", b=P),
                                      AX.X, ALU.add).then_inc(s0_reduced, 1)
                    dve.wait_ge(s0_reduced, n + 1)
                    if q == 0:
                        dve.nop().then_inc(s0_added, 1)
                    else:
                        dve.tensor_tensor(s0_acc[:], s0_acc[:], s0_quad[:], ALU.add).then_inc(s0_added, 1)

            def post(g, s):
                for t in range(NBLK):
                    if s == P2_SLOT[t] - BLK_AHEAD:
                        if t == 0:
                            dve.wait_ge(x0r_in, 2 * NBLK * 16 * (g + 1))
                        if t >= BLK_RING:
                            dve.wait_ge(p2_ready, NBLK * g + t + 1 - BLK_RING)
                        shape = [P, BLK, FX]
                        dve.tensor_tensor(blk[:, t % BLK_RING], x0r[:, t, :].unsqueeze(1).broadcast_to(shape),
                                          mask[:].unsqueeze(2).broadcast_to(shape), ALU.mult).then_inc(blk_ready, 1)

            def body(j):
                dve.wait_ge(x_next_ready, j + 1)
                reach(dve, dve_part, ND * j)
                dve.tensor_copy(x_dve[:], x_next[:]).then_inc(x_dve_ready, 1)
                dve.wait_ge(x_dve_ready, j + 1)
                for s in range(SLOTS):
                    i, u = divmod(s, BANKS)
                    if u not in ACT_BANKS[i % 2]:
                        if u == 0:
                            reach(dve, x2_ready, j * TILES + i - 1)
                        dve.wait_ge(u_ready, j * SLOTS + s + 1)
                        for k, f in enumerate(bank_features(u)):
                            m = features_of(False, i, u) + k
                            acc = parts[:, i % 2, features_of(True, i) + m % 2, :]
                            prod = u_ps[s % RING][:, k * M:(k + 1) * M]
                            if m < 2:
                                dve.tensor_scalar(acc, prod, x_dve[:, i, f:f + 1], None, ALU.mult).then_inc(dve_part, 1)
                            else:
                                dve.wait_ge(dve_part, j * ND + features_before(False, i) + m - 1)
                                dve.scalar_tensor_tensor(acc, prod, x_dve[:, i, f:f + 1], acc,
                                                         ALU.mult, ALU.add).then_inc(dve_part, 1)
                    if s == XS_LO_SLOT and has_next(j):
                        split_x0_lo(j + 1)
                    if s == S0_COPY_SLOT:
                        reach(dve, h1_ready, j)
                        dve.wait_ge(s0_added, (j + 1) * QUADS)
                        dve.tensor_copy(s0_in[:], s0_acc[:]).then_inc(s0_in_ready, 1)
                    ahead(j, s)
                    if has_prev(j):
                        post(j - 1, s)

            dve.wait_ge(w1_hi_ready, 1)
            dve.tensor_tensor(w1_lo[:], w1_stage, w1_hi[:].bitcast(FP32), ALU.subtract).then_inc(w1_lo_ready, 1)
            dve.wait_ge(v_in, 16 * 2 * RPC)
            for c in range(CHUNKS):
                dve.tensor_tensor(vs[0:rows_of(c), c, :], va[0:rows_of(c), c, :], vb[0:rows_of(c), c, :], ALU.add).then_inc(v_prep, 1)
            dve.wait_ge(v_prep, CHUNKS)
            dve.tensor_scalar(vs[0:F, 0, :], vs[0:F, 0, :], 0.5, None, ALU.mult).then_inc(v_prep, 1)
            dve.wait_ge(v_prep, CHUNKS + 1)
            dve.nop().then_inc(v_prep, 1)
            dve.wait_ge(v_hi_ready, 1)
            for c in range(CHUNKS):
                last = dve.tensor_tensor(v_lo[0:rows_of(c), c, :], vs[0:rows_of(c), c, :],
                                         v_hi[0:rows_of(c), c, :].bitcast(FP32), ALU.subtract)
            last.then_inc(v_lo_ready, 1)
            split_x0_lo(0)
            for s in before_body0():
                ahead(0, s)
            bodies(dve, body)
            dve.wait_ge(x2_ready, GROUPS * TILES - 1)
            add_up(dve, GROUPS - 1, TILES - 1)
            for s in range(SLOTS):
                post(GROUPS - 1, s)


def selection():
    s = np.zeros((2 * F, 1 + CHUNKS, RPC * F), np.float32)
    for i in range(1 + CHUNKS):
        for r in range(RPC):
            for f in range(F):
                g = f if i == 0 else (f + RPC * (i - 1) + r) % F
                s[g, i, F * r + f] = s[F + g, i, F * r + f] = 1.0
    return s.reshape(2 * F, -1)


def kernel(**inputs):
    import concourse.bacc as bacc
    from concourse.bass_utils import run_bass_kernel_spmd

    nc = bacc.Bacc("TRN2", target_bir_lowering=False, num_devices=1)
    arrays = {}

    def given(name, a):
        a = np.ascontiguousarray(a)
        arrays[name] = a
        return nc.dram_tensor(name, a.shape, mybir.dt.from_np(a.dtype), kind="ExternalInput").ap()

    ids = given("ids", inputs["ids"])
    dense = given("dense_ctx", inputs["dense_ctx"])
    tables = [given(f"tbl_{f}", inputs[f"tbl_{f}"]) for f in range(F)]
    w0, w1, w2 = (given(f"L0_rec_f{k}", inputs[f"L0_rec_f{k}"]) for k in range(3))
    wt1, bt1, wt2, bt2, wt3 = (given(k, inputs[k]) for k in ("W_top1", "b_top1", "W_top2", "b_top2", "W_top3"))
    c_ident = given("c_ident", np.eye(P, dtype=np.float32))
    c_sel = given("c_sel", selection())
    part = np.arange(P)
    c_mask = given("c_mask", ((part[:, None] // (D // 2)) % BLK == np.arange(BLK)[None, :]).astype(np.float32))
    y = nc.dram_tensor("y", (B, 1), FP32, kind="ExternalOutput").ap()
    build(nc, ids, dense, tables, w0, w1, w2, wt1, bt1, wt2, bt2, wt3, c_ident, c_sel, c_mask, y)
    r = run_bass_kernel_spmd(nc, [arrays], core_ids=[0])
    return r.results[0]["y"]
```
